# Optimizing a Trainium2 kernel written in Bass

```python
import numpy as np
import jax
import jax.numpy as jnp

def _softmax(x, axis=-1):
    return jax.nn.softmax(x, axis=axis)

def _gelu(x):
    return jax.nn.gelu(x, approximate=True)

def _silu(x):
    return jax.nn.silu(x)

def _sigmoid(x):
    return jax.nn.sigmoid(x)

def _layernorm(x, axis=-1, eps=1e-05):
    m = jnp.mean(x, axis=axis, keepdims=True)
    v = jnp.var(x, axis=axis, keepdims=True)
    return (x - m) / jnp.sqrt(v + eps)

def _scatter_add(tgt, idx, src, axis=0):
    return tgt.at[idx].add(src)

def _segment_sum(src, seg, n):
    return jax.ops.segment_sum(src, seg, n)
kernel_name = 'mk_gnn_preln_d4_gnn_r32_dea658'

def setup_inputs(seed: int=0):
    np.random.seed(seed)
    _w = jnp.asarray

    def _rec_inputs():
        import jax
        import jax.numpy as jnp
        _gk = jax.random.key(seed)
        x = -0.0003713 + 1 * jax.random.normal(jax.random.fold_in(_gk, 1), (3125, 256), jnp.float32)
        src = jax.random.randint(jax.random.fold_in(_gk, 2), (50000,), 0, 3125, jnp.int32)
        dst = jax.random.randint(jax.random.fold_in(_gk, 3), (50000,), 0, 3125, jnp.int32)
        _o = jnp.argsort(dst, stable=True)
        src = src[_o]
        dst = dst[_o]
        edge_type_8 = jax.random.randint(jax.random.fold_in(_gk, 13), (50000,), 0, 8, jnp.int32)
        edge_weight = jax.random.uniform(jax.random.fold_in(_gk, 14), (50000,), jnp.float32, 0.0, 1)
        return (x, src, dst, edge_type_8, edge_weight)
    x, src, dst, edge_type_8, edge_weight = _rec_inputs()

    def _L0_gnn_setup():
        import jax, jax.numpy as jnp
        import numpy as np
        N_NODES = 50000
        N_EDGES = 25000
        D = 256

        def _mean_aggregate(x, src, tgt, num_nodes):
            summed = jax.ops.segment_sum(x[src], tgt, num_segments=num_nodes)
            count = jax.ops.segment_sum(jnp.ones((src.shape[0],), x.dtype), tgt, num_segments=num_nodes)
            return summed / jnp.maximum(count, 1.0)[:, None]

        def _sage_conv(x, src, tgt, W_l, b, W_r):
            agg = _mean_aggregate(x, src, tgt, x.shape[0])
            return agg @ W_l + b + x @ W_r
        key = jax.random.key(seed)
        ks = jax.random.split(key, 8)
        s = 1.0 / np.sqrt(D)
        x = jax.random.normal(ks[0], (N_NODES, D), dtype=jnp.float32)
        edge_index = jax.random.randint(ks[1], (2, N_EDGES), 0, N_NODES, dtype=jnp.int64)
        return {'x': x, 'edge_index': edge_index, 'W1_l': jax.random.normal(ks[2], (D, D), dtype=jnp.float32) * s, 'b1': jnp.zeros((D,), dtype=jnp.float32), 'W1_r': jax.random.normal(ks[3], (D, D), dtype=jnp.float32) * s, 'W2_l': jax.random.normal(ks[4], (D, D), dtype=jnp.float32) * s, 'b2': jnp.zeros((D,), dtype=jnp.float32), 'W2_r': jax.random.normal(ks[5], (D, D), dtype=jnp.float32) * s}
    _L0_gnn_all = _L0_gnn_setup()
    _L0_gnn_in = {k: v for k, v in _L0_gnn_all.items() if k in ('W1_l', 'b1', 'W1_r', 'W2_l', 'b2', 'W2_r')}
    del _L0_gnn_all

    def _L1_gnn_setup():
        import jax, jax.numpy as jnp
        import numpy as np
        N_NODES = 50000
        N_EDGES = 25000
        N_REL = 8
        HID = 256
        N_BASES = 30
        N_LAYERS = 2
        key = jax.random.key(seed)
        ks = jax.random.split(key, 6)
        edge_index = jax.random.randint(ks[0], (2, N_EDGES), 0, N_NODES)
        edge_type = jax.random.randint(ks[1], (N_EDGES,), 0, N_REL)
        s_w = (6.0 / (HID + HID)) ** 0.5
        emb = jax.random.normal(ks[2], (N_NODES, HID), dtype=jnp.float32) * 0.05
        bases = jax.random.uniform(ks[3], (N_LAYERS, N_BASES, HID, HID), dtype=jnp.float32, minval=-s_w, maxval=s_w)
        coeffs = jax.random.uniform(ks[4], (N_LAYERS, N_REL, N_BASES), dtype=jnp.float32, minval=-0.4, maxval=0.4)
        self_loops = jax.random.uniform(ks[5], (N_LAYERS, HID, HID), dtype=jnp.float32, minval=-s_w, maxval=s_w)
        return {'edge_index': edge_index, 'edge_type': edge_type, 'num_nodes': N_NODES, 'emb': emb, 'bases': bases, 'coeffs': coeffs, 'self_loops': self_loops}
    _L1_gnn_all = _L1_gnn_setup()
    _L1_gnn_in = {k: v for k, v in _L1_gnn_all.items() if k in ('bases', 'coeffs', 'self_loops')}
    del _L1_gnn_all

    def _L2_gnn_setup():
        import jax, jax.numpy as jnp
        import numpy as np
        N_NODES = 3125
        N_EDGES = 100000
        DIM = 256
        PRESERVE = 0.1

        def _gcn_conv(x, W, b, src, dst, ew, n_nodes):
            loop = jnp.arange(n_nodes, dtype=src.dtype)
            src2 = jnp.concatenate([src, loop])
            dst2 = jnp.concatenate([dst, loop])
            ew2 = jnp.concatenate([ew, jnp.ones((n_nodes,), dtype=ew.dtype)])
            deg = jax.ops.segment_sum(ew2, dst2, num_segments=n_nodes)
            dinv = jnp.where(deg > 0, jax.lax.rsqrt(jnp.maximum(deg, 1e-30)), 0.0)
            norm = dinv[src2] * ew2 * dinv[dst2]
            xw = x @ W
            msg = xw[src2] * norm[:, None]
            out = jax.ops.segment_sum(msg, dst2, num_segments=n_nodes)
            return out + b
        key = jax.random.key(seed)
        k = jax.random.split(key, 8)
        skill_embed = jax.random.normal(k[0], (N_NODES, DIM), dtype=jnp.float32)
        adj_list = jax.random.randint(k[1], (2, N_EDGES), 0, N_NODES, dtype=jnp.int64)
        edge_attr = jax.random.uniform(k[2], (N_EDGES,), dtype=jnp.float32)
        s = 1.0 / np.sqrt(DIM)
        W1 = jax.random.uniform(k[3], (DIM, DIM), dtype=jnp.float32, minval=-s, maxval=s)
        b1 = jnp.zeros((DIM,), dtype=jnp.float32)
        W2 = jax.random.uniform(k[4], (DIM, DIM), dtype=jnp.float32, minval=-s, maxval=s)
        b2 = jnp.zeros((DIM,), dtype=jnp.float32)
        return {'skill_embed': skill_embed, 'adj_list': adj_list, 'edge_attr': edge_attr, 'W1': W1, 'b1': b1, 'W2': W2, 'b2': b2}
    _L2_gnn_all = _L2_gnn_setup()
    _L2_gnn_in = {k: v for k, v in _L2_gnn_all.items() if k in ('W1', 'b1', 'W2', 'b2')}
    del _L2_gnn_all

    def _L3_gnn_setup():
        import jax, jax.numpy as jnp
        import numpy as np
        N = 3125
        E = 50000
        IN_FEATS = 256
        OUT_FEATS = 256
        MAXK = 32

        def _maxk(x, k):
            _, idx = jax.lax.top_k(x, k)
            rows = jnp.arange(x.shape[0])[:, None]
            mask = jnp.zeros_like(x).at[rows, idx].set(1.0)
            return x * mask
        key = jax.random.key(seed)
        k1, k2, k3, k4, k5 = jax.random.split(key, 5)
        feat = jax.random.normal(k1, (N, IN_FEATS), dtype=jnp.float32)
        W_self = jax.random.normal(k2, (IN_FEATS, OUT_FEATS), dtype=jnp.float32) * (1.0 / np.sqrt(IN_FEATS))
        W_neigh = jax.random.normal(k3, (IN_FEATS, OUT_FEATS), dtype=jnp.float32) * (1.0 / np.sqrt(IN_FEATS))
        src = jax.random.randint(k4, (E,), 0, N, dtype=jnp.int64)
        dst = jax.random.randint(k5, (E,), 0, N, dtype=jnp.int64)
        return {'feat': feat, 'W_self': W_self, 'W_neigh': W_neigh, 'src': src, 'dst': dst}
    _L3_gnn_all = _L3_gnn_setup()
    _L3_gnn_in = {k: v for k, v in _L3_gnn_all.items() if k in ('W_self', 'W_neigh')}
    del _L3_gnn_all
    return {'x': x, 'src': src, 'dst': dst, 'edge_type_8': edge_type_8, 'edge_weight': edge_weight, 'L0_gnn_W1_l': _L0_gnn_in['W1_l'], 'L0_gnn_b1': _L0_gnn_in['b1'], 'L0_gnn_W1_r': _L0_gnn_in['W1_r'], 'L0_gnn_W2_l': _L0_gnn_in['W2_l'], 'L0_gnn_b2': _L0_gnn_in['b2'], 'L0_gnn_W2_r': _L0_gnn_in['W2_r'], 'L1_gnn_bases': _L1_gnn_in['bases'], 'L1_gnn_coeffs': _L1_gnn_in['coeffs'], 'L1_gnn_self_loops': _L1_gnn_in['self_loops'], 'L2_gnn_W1': _L2_gnn_in['W1'], 'L2_gnn_b1': _L2_gnn_in['b1'], 'L2_gnn_W2': _L2_gnn_in['W2'], 'L2_gnn_b2': _L2_gnn_in['b2'], 'L3_gnn_W_self': _L3_gnn_in['W_self'], 'L3_gnn_W_neigh': _L3_gnn_in['W_neigh']}

def reference(x, src, dst, edge_type_8, edge_weight, L0_gnn_W1_l, L0_gnn_b1, L0_gnn_W1_r, L0_gnn_W2_l, L0_gnn_b2, L0_gnn_W2_r, L1_gnn_bases, L1_gnn_coeffs, L1_gnn_self_loops, L2_gnn_W1, L2_gnn_b1, L2_gnn_W2, L2_gnn_b2, L3_gnn_W_self, L3_gnn_W_neigh):
    import jax
    import jax.numpy as jnp

    def _L0_gnn_ref(x, edge_index, W1_l, b1, W1_r, W2_l, b2, W2_r):
        import jax, jax.numpy as jnp
        import numpy as np
        N_NODES = 50000
        N_EDGES = 25000
        D = 256

        def _mean_aggregate(x, src, tgt, num_nodes):
            summed = jax.ops.segment_sum(x[src], tgt, num_segments=num_nodes)
            count = jax.ops.segment_sum(jnp.ones((src.shape[0],), x.dtype), tgt, num_segments=num_nodes)
            return summed / jnp.maximum(count, 1.0)[:, None]

        def _sage_conv(x, src, tgt, W_l, b, W_r):
            agg = _mean_aggregate(x, src, tgt, x.shape[0])
            return agg @ W_l + b + x @ W_r
        src, tgt = (edge_index[0], edge_index[1])
        h = jax.nn.relu(_sage_conv(x, src, tgt, W1_l, b1, W1_r))
        return _sage_conv(h, src, tgt, W2_l, b2, W2_r)

    def _L1_gnn_ref(edge_index, edge_type, num_nodes, emb, bases, coeffs, self_loops):
        import jax, jax.numpy as jnp
        import numpy as np
        N_NODES = 50000
        N_EDGES = 25000
        N_REL = 8
        HID = 256
        N_BASES = 30
        N_LAYERS = 2
        src, dst = (edge_index[0], edge_index[1])
        deg = jax.ops.segment_sum(jnp.ones_like(dst, dtype=emb.dtype), dst, num_segments=num_nodes)
        deg_inv = 1.0 / jnp.maximum(deg, 1.0)
        x = emb
        n_layers = bases.shape[0]
        for l in range(n_layers):
            W = jnp.einsum('rb,bio->rio', coeffs[l], bases[l])
            h = jnp.einsum('ni,rio->rno', x, W)
            msg = h[edge_type, src] * deg_inv[dst][:, None]
            agg = jax.ops.segment_sum(msg, dst, num_segments=num_nodes)
            x_new = agg + x @ self_loops[l]
            if l < n_layers - 1:
                x_new = jax.nn.relu(x_new)
            x = x_new
        return x

    def _L2_gnn_ref(skill_embed, adj_list, edge_attr, W1, b1, W2, b2):
        import jax, jax.numpy as jnp
        import numpy as np
        N_NODES = 3125
        N_EDGES = 100000
        DIM = 256
        PRESERVE = 0.1

        def _gcn_conv(x, W, b, src, dst, ew, n_nodes):
            loop = jnp.arange(n_nodes, dtype=src.dtype)
            src2 = jnp.concatenate([src, loop])
            dst2 = jnp.concatenate([dst, loop])
            ew2 = jnp.concatenate([ew, jnp.ones((n_nodes,), dtype=ew.dtype)])
            deg = jax.ops.segment_sum(ew2, dst2, num_segments=n_nodes)
            dinv = jnp.where(deg > 0, jax.lax.rsqrt(jnp.maximum(deg, 1e-30)), 0.0)
            norm = dinv[src2] * ew2 * dinv[dst2]
            xw = x @ W
            msg = xw[src2] * norm[:, None]
            out = jax.ops.segment_sum(msg, dst2, num_segments=n_nodes)
            return out + b
        src, dst = (adj_list[0], adj_list[1])
        n = skill_embed.shape[0]
        temp = skill_embed
        out = _gcn_conv(skill_embed, W1, b1, src, dst, edge_attr, n)
        temp = (1.0 - PRESERVE) * out + PRESERVE * temp
        out = _gcn_conv(temp, W2, b2, src, dst, edge_attr, n)
        temp = (1.0 - PRESERVE) * out + PRESERVE * temp
        return temp

    def _L3_gnn_ref(feat, W_self, W_neigh, src, dst):
        import jax, jax.numpy as jnp
        import numpy as np
        N = 3125
        E = 50000
        IN_FEATS = 256
        OUT_FEATS = 256
        MAXK = 32

        def _maxk(x, k):
            _, idx = jax.lax.top_k(x, k)
            rows = jnp.arange(x.shape[0])[:, None]
            mask = jnp.zeros_like(x).at[rows, idx].set(1.0)
            return x * mask
        n = feat.shape[0]
        h_self = feat @ W_self
        h_neigh = feat @ W_neigh
        h_sparse = _maxk(h_neigh, MAXK)
        msg = h_sparse[src]
        summed = jax.ops.segment_sum(msg, dst, num_segments=n)
        deg = jax.ops.segment_sum(jnp.ones((src.shape[0],), dtype=feat.dtype), dst, num_segments=n)
        neigh = summed / jnp.maximum(deg, 1.0)[:, None]
        return h_self + neigh
    edge_index = jnp.stack([src, dst])
    h = jnp.maximum(_layernorm(x, axis=-1), 0.0)
    x = x + _L0_gnn_ref(h, edge_index, L0_gnn_W1_l, L0_gnn_b1, L0_gnn_W1_r, L0_gnn_W2_l, L0_gnn_b2, L0_gnn_W2_r)
    h = jnp.maximum(_layernorm(x, axis=-1), 0.0)
    x = x + _L1_gnn_ref(edge_index, edge_type_8, 3125, h, L1_gnn_bases, L1_gnn_coeffs, L1_gnn_self_loops)
    h = jnp.maximum(_layernorm(x, axis=-1), 0.0)
    x = x + _L2_gnn_ref(h, edge_index, edge_weight, L2_gnn_W1, L2_gnn_b1, L2_gnn_W2, L2_gnn_b2)
    h = jnp.maximum(_layernorm(x, axis=-1), 0.0)
    x = x + _L3_gnn_ref(h, L3_gnn_W_self, L3_gnn_W_neigh, src, dst)
    return x

_drawn_inputs = setup_inputs


def setup_inputs(seed=0):
    import zlib

    import numpy as np

    out = dict(_drawn_inputs(seed))
    spreads = {'L0_gnn_b1': (0.0, 0.1),
     'L0_gnn_b2': (0.0, 0.1),
     'L2_gnn_b1': (0.0, 0.1),
     'L2_gnn_b2': (0.0, 0.1)}
    factors = {}
    for name, (base, spread) in spreads.items():
        noise = np.random.default_rng([zlib.crc32(name.encode()), seed]).standard_normal(out[name].shape)
        drawn = base * np.exp(spread * noise) if base else spread * noise
        out[name] = jnp.asarray(drawn.astype(out[name].dtype))
    for name, factor in factors.items():
        out[name] = (out[name] * factor).astype(out[name].dtype)
    return out
```

```python
import concourse.bass as bass
from concourse import mybir
from contextlib import ExitStack

P = 128


def gnn_program(nc, t, out):
    fp32 = mybir.dt.float32
    i32 = mybir.dt.int32
    ALU = mybir.AluOpType
    ACT = mybir.ActivationFunctionType
    DVE = mybir.EngineType.DVE
    ds = bass.ds

    NODES, D = t["x"].shape
    EDGES = t["src"].shape[0]
    LAYERS, BASES = t["L1_gnn_bases"].shape[:2]
    RELS = t["L1_gnn_coeffs"].shape[1]
    EPS = 1e-5
    PRESERVE = 0.1
    MAXK = 32
    KC = D // P
    BLOCKS = -(-NODES // P)
    NB = BLOCKS + BLOCKS % 2
    LAST = NODES - (BLOCKS - 1) * P
    U = 16
    TURNS = -(-(EDGES // P + BLOCKS) // U)
    TILES = TURNS * U
    TC = 4
    TP = TILES // TC
    RING = 8
    BANKS = 4
    LEAD = 4
    AW = 260
    EP = max(p for p in range(1, P + 1) if EDGES % p == 0)
    AGGS = 7
    assert TURNS == NB and TP <= P and BLOCKS < NB

    ctx = ExitStack()
    with ctx:
        def sb(name, shape, dt=fp32):
            return ctx.enter_context(nc.sbuf_tensor(name, shape, dt))

        def sem(name):
            return ctx.enter_context(nc.semaphore(name))

        def dram(name, shape, dt=fp32):
            return nc.dram_tensor(name, shape, dt, kind="Internal").ap()

        node_table = [dram(f"node_table{a}", [NB * P, D]) for a in range(AGGS)]
        rel_table = [dram(f"rel_table{l}", [NB * P, RELS * D]) for l in range(LAYERS)]
        rel_weight = [dram(f"rel_weight{l}", [P // BASES * RELS, D * D // (P // BASES)]) for l in range(LAYERS)]
        tile_acc_dram = dram("tile_acc_dram", [TP, TC], i32)

        X = sb("X", [P, NB * D])
        H = sb("H", [P, NB * D])
        SELF = sb("SELF", [P, NB * D])
        acc = sb("acc", [P, NB * AW])
        mv = sb("mv", [P, NB * 2])
        mv_pair = sb("mv_pair", [P, 2, 2])
        rstd = sb("rstd", [P, NB])
        shift = sb("shift", [P, NB])
        rdeg = sb("rdeg", [P, NB])
        dinv = sb("dinv", [P, NB])
        small = sb("small", [P, 2, NB])
        src_idx = sb("src_idx", [P, TILES + U], i32)
        rel_idx = sb("rel_idx", [P, TILES + U], i32)
        target = sb("target", [P, TILES])
        ones_w = sb("ones_w", [P, TILES, 2])
        tile_acc = sb("tile_acc", [1, TILES], i32)
        idx_ring = sb("idx_ring", [P, U], i32)
        rows = sb("rows", [P, RING, D])
        match = sb("match", [P, RING, P])
        WNAMES = ["L0_gnn_W1_l", "L0_gnn_W1_r", "L0_gnn_W2_l", "L0_gnn_W2_r", "L2_gnn_W1", "L2_gnn_W2",
                  "L3_gnn_W_self", "L3_gnn_W_neigh"]
        W = {n: sb(n.lower(), [P, KC, D]) for n in WNAMES}
        for l in range(LAYERS):
            W[f"self{l}"] = sb(f"self_w{l}", [P, KC, D])
        Wrel = sb("wrel", [P, KC, RELS * D])
        bias_row = sb("bias_row", [1, 2, D])
        bias = sb("bias", [P, 2, D])
        stage = sb("stage", [P, 2, D])
        turned_sb = sb("turned_sb", [P, 2, D])
        tmp = sb("tmp", [P, 2, D])
        tmp2 = sb("tmp2", [P, 2, D])
        top8 = sb("top8", [P, 8])
        stats = sb("stats", [P, 2, 6])
        self_stage = sb("self_stage", [P, D])
        self_turned = sb("self_turned", [P, D])
        rel_rows = sb("rel_rows", [P, 2, RELS * D])
        ident = sb("ident", [P, P])
        column = sb("column", [P, P])
        ones = sb("ones", [P, P])
        tile_no = sb("tile_no", [P, TC])
        QB = P // BASES
        BPC = 1024
        QL = D * D // QB
        coef = sb("coef", [QB * BASES, LAYERS, QB * RELS])
        base_in = Wrel[0:QB * BASES, 0, 0:2 * BPC].rearrange("p (a m) -> p a m", a=2)
        base_out = Wrel[0:QB * RELS, 1, 0:2 * BPC].rearrange("p (a m) -> p a m", a=2)
        dst_i = SELF[0:EP, 0:EDGES // EP].bitcast(i32)
        dst_f = SELF[0:EP, 512:512 + EDGES // EP]
        below = SELF[0:EP, 1024:1024 + EDGES // EP]
        FIELDS = 4
        rec = [SELF[0:TP, 1536 + f * TC * P:1536 + (f + 1) * TC * P] for f in range(FIELDS)]
        prep = rel_rows.rearrange("p a w -> p (a w)")
        rec_f = [prep[0:TP, f * TC * P:(f + 1) * TC * P] for f in range(FIELDS)]
        valid = prep[0:TP, FIELDS * TC * P:(FIELDS + 1) * TC * P]
        cnt = sb("cnt", [P, NB])
        cum = sb("cum", [P, NB])
        runs = sb("runs", [P, 8, NB])
        runs_i = sb("runs_i", [P, NB], i32)
        cut = sb("cut", [P, 8, TC])
        start_i = sb("start_i", [P, TC], i32)
        acc_i = sb("acc_i", [P, TC], i32)

        ps = ctx.enter_context(nc.psum_tensor("ps", [P, 8, 512], fp32))

        nodes_in = sem("nodes_in")
        weights_in = sem("weights_in")
        coef_in = sem("coef_in")
        dst_in = sem("dst_in")
        bases_in = [sem(f"bases_in{i}") for i in range(2)]
        bases_mixed = sem("bases_mixed")
        bases_copied = sem("bases_copied")
        bases_out = [sem(f"bases_out{i}") for i in range(2)]
        wrel_in = sem("wrel_in")
        const_made = sem("const_made")
        counted = sem("counted")
        cum_made = sem("cum_made")
        starts_made = sem("starts_made")
        tile_acc_out = sem("tile_acc_out")
        tile_acc_in = sem("tile_acc_in")
        fields_in = sem("fields_in")
        fields_made = sem("fields_made")
        fields_turned = sem("fields_turned")
        slots_made = sem("slots_made")
        dve_step = sem("dve_step")
        act_step = sem("act_step")
        pool_step = sem("pool_step")
        acc_zeroed = sem("acc_zeroed")
        acc_read = sem("acc_read")
        table_out = sem("table_out")
        idx_ready = sem("idx_ready")
        gathered = [sem(f"gathered{i}") for i in range(RING)]
        match_ready = sem("match_ready")
        tile_summed = sem("tile_summed")
        tile_added = sem("tile_added")
        self_staged = sem("self_staged")
        self_transposed = sem("self_transposed")
        self_copied = sem("self_copied")
        self_multiplied = sem("self_multiplied")
        self_saved = sem("self_saved")
        staged = sem("staged")
        transposed = sem("transposed")
        turned = sem("turned")
        multiplied = sem("multiplied")
        block_done = sem("block_done")
        var_ready = sem("var_ready")
        root_ready = sem("root_ready")
        norm_ready = sem("norm_ready")
        normed = sem("normed")
        pre_relu = sem("pre_relu")
        rel_done = sem("rel_done")
        rel_low_saved = sem("rel_low_saved")
        rel_high_saved = sem("rel_high_saved")
        rel_stored = [sem(f"rel_stored{i}") for i in range(2)]
        scaled = sem("scaled")
        out_sent = sem("out_sent")

        block = ctx.enter_context(nc.Block())

        SELF_W = {0: "L0_gnn_W1_r", 1: "L0_gnn_W2_r", 2: "self0", 3: "self1"}
        SELF_BASE = {a: n * NB for n, a in enumerate(SELF_W)}
        PROJECT_W = {0: "L0_gnn_W1_l", 1: "L0_gnn_W2_l", 4: "L2_gnn_W1", 5: "L2_gnn_W2"}
        TURN_ORDER = ["p0", "p1", "r0", "r1", "p4", "p5", "m"]
        TURN_BASE = {n: k * NB for k, n in enumerate(TURN_ORDER)}
        MUL_ORDER = ["p0", "p1", "p4", "p5", "m"]
        MUL_BASE = {n: k * NB for k, n in enumerate(MUL_ORDER)}
        NORM = {1: 1, 3: 2, 5: 3}
        PAIRS = NB // 2
        TABLE_DMAS = [PAIRS, PAIRS, 0, 0, PAIRS, PAIRS, PAIRS]
        TABLE_SUM = [16 * sum(TABLE_DMAS[:a + 1]) for a in range(AGGS)]

        def blk(tensor, n, w=D):
            return tensor[:, ds(n * D, w)]

        def pair(tensor, i):
            return tensor[:, ds(i * (2 * D), 2 * D)]

        def rows_of(table, i, w):
            return table[ds(i * (2 * P), 2 * P), :].rearrange("(b p) w -> p b w", p=P)

        class Chain:

            def __init__(self, eng, s):
                self.eng, self.sem, self.n, self.i, self.per = eng, s, 0, None, 0

            def __call__(self, ins):
                ins.then_inc(self.sem, 1)
                self.n += 1
                self.eng.wait_ge(self.sem, self.n if self.i is None else self.i * self.per + self.n)

            def loop(self, lo, hi, per, body):
                with self.eng.Fori(lo, hi) as i:
                    self.i, self.per = i, per
                    start = self.n
                    self.n -= lo * per
                    body(i)
                    assert self.n == start - lo * per + per, (self.n - start + lo * per, per)
                    self.i = None
                    self.n = start + (hi - lo) * per

        @block.sync
        def _(sp):
            full = BLOCKS - 1
            sp.dma_start(dst_i, t["dst"].rearrange("(p t) -> p t", p=EP)).then_inc(dst_in, 16)
            sp.dma_start(X[:, 0:full * D].rearrange("p (b w) -> p b w", w=D),
                         t["x"][0:full * P, :].rearrange("(b p) w -> p b w", p=P)).then_inc(nodes_in, 16)
            sp.wait_ge(const_made, 1)
            sp.dma_start(X[0:LAST, full * D:BLOCKS * D], t["x"][full * P:NODES, :]).then_inc(nodes_in, 16)
            sp.wait_ge(const_made, 2)
            for l in range(LAYERS):
                for q in range(QB):
                    sp.dma_start(coef[q * BASES:(q + 1) * BASES, l, q * RELS:(q + 1) * RELS],
                                 t["L1_gnn_coeffs"][l].rearrange("r b -> b r"),
                                 allow_slow_non_contiguous=True).then_inc(coef_in, 16)
            pieces = QL // BPC
            for l in range(LAYERS):
                flat = t["L1_gnn_bases"][l].rearrange("b i o -> b (i o)")
                for c in range(pieces):
                    n = l * pieces + c
                    if n >= 2:
                        sp.wait_ge(bases_mixed, 2 * (n - 1))
                    for q in range(QB):
                        sp.dma_start(base_in[q * BASES:(q + 1) * BASES, n % 2, :],
                                     flat[:, q * QL + c * BPC:q * QL + (c + 1) * BPC]).then_inc(bases_in[n % 2], 16)
            for n_, w in enumerate(WNAMES):
                sp.dma_start(W[w][:, :, :], t[w].rearrange("(c p) o -> p c o", p=P)).then_inc(weights_in, 16)
            for l in range(LAYERS):
                sp.dma_start(W[f"self{l}"][:, :, :],
                             t["L1_gnn_self_loops"][l].rearrange("(c p) o -> p c o", p=P)).then_inc(weights_in, 16)
            for k in range(2):
                sp.dma_start(bias_row[0:1, k, :], t[f"L0_gnn_b{k + 1}"].rearrange("(a n) -> a n", a=1)).then_inc(weights_in, 16)
                sp.dma_start(bias[:, k, :], t[f"L2_gnn_b{k + 1}"].partition_broadcast(P)).then_inc(weights_in, 16)
            def store_pairs(a, ready, base):
                with sp.Fori(0, PAIRS) as i:
                    sp.wait_ge(ready, i * 2 + (base + 2))
                    sp.dma_start(rows_of(node_table[a], i, D),
                                 pair(H, i).rearrange("p (b w) -> p b w", w=D)).then_inc(table_out, 16)

            store_pairs(0, normed, 0)
            sp.wait_ge(starts_made, 1)
            sp.dma_start(tile_acc_dram[:, :], acc_i[0:TP, :]).then_inc(tile_acc_out, 16)
            sp.wait_ge(tile_acc_out, 16)
            sp.dma_start(tile_acc[0:1, :], tile_acc_dram.rearrange("(a p) c -> a (p c)", a=1)).then_inc(tile_acc_in, 16)
            for s in range(2):
                sp.wait_ge(bases_out[s], 16 * (LAYERS * pieces // 2))
            def load_wrel(l):
                rpq = QL // D
                for q in range(QB):
                    at = q * rpq % P
                    sp.dma_start(Wrel[at:at + rpq, q * rpq // P, :].rearrange("p (r o) -> p r o", r=RELS),
                                 rel_weight[l][q * RELS:(q + 1) * RELS, :].rearrange("r (i o) -> i r o", o=D)).then_inc(wrel_in, 16)

            load_wrel(0)
            store_pairs(1, block_done, 0)

            def store_rel(l):
                for_base = l * NB
                with sp.Fori(0, PAIRS) as i:
                    for u in range(2):
                        sp.wait_ge(rel_low_saved, i * 2 + (for_base + u + 1))
                        sp.wait_ge(rel_high_saved, i * 2 + (for_base + u + 1))
                        sp.dma_start(rel_table[l][ds(i * (2 * P) + u * P, P), :], rel_rows[:, u, :]).then_inc(rel_stored[u], 16)

            store_rel(0)
            sp.wait_ge(rel_done, 2 * NB)
            load_wrel(1)
            store_rel(1)

            def store_tmp(a, base):
                with sp.Fori(0, PAIRS) as i:
                    sp.wait_ge(scaled, i * 2 + (base + 2))
                    sp.dma_start(rows_of(node_table[a], i, D), tmp2[:, :, :]).then_inc(table_out, 16)

            store_tmp(4, 0)
            store_tmp(5, NB)
            store_tmp(6, 2 * NB)
            with sp.Fori(0, full // 2) as i:
                sp.wait_ge(block_done, i * 2 + (NB + 2))
                sp.dma_start(rows_of(out, i, D), pair(X, i).rearrange("p (b w) -> p b w", w=D)).then_inc(out_sent, 16)
            sp.wait_ge(block_done, NB + BLOCKS)
            sp.dma_start(out[full * P:NODES, :], X[0:LAST, full * D:BLOCKS * D]).then_inc(out_sent, 16)
            sp.wait_ge(out_sent, 16 * (full // 2 + 1))

        @block.gpsimd
        def _(pool):
            pool.memset(ident[:, :], 0.0).then_inc(pool_step, 1)
            pool.iota(column[:, :], pattern=[[1, P]], base=0, channel_multiplier=0,
                      allow_small_or_imprecise_dtypes=True).then_inc(pool_step, 1)
            pool.iota(tile_no[:, :], pattern=[[1, TC]], base=0, channel_multiplier=TC,
                      allow_small_or_imprecise_dtypes=True).then_inc(pool_step, 1)
            pool.wait_ge(pool_step, 1)
            pool.affine_select(out=ident[:, :], in_=ident[:, :], compare_op=ALU.not_equal, fill=1.0,
                               base=0, pattern=[[-1, P]], channel_multiplier=1).then_inc(pool_step, 1)
            pool.memset(acc[:, :], 0.0).then_inc(acc_zeroed, 1)
            pool.wait_ge(starts_made, 2)
            for f, name in enumerate(["dst", "src", "edge_type_8", "edge_weight"]):
                for c in range(TC):
                    o = rec[f][:, c * P:(c + 1) * P]
                    pool.indirect_dma_start(
                        out=o if name == "edge_weight" else o.bitcast(i32), out_offset=None,
                        in_=t[name].rearrange("(a b) -> a b", a=1),
                        in_offset=bass.IndirectOffsetOnAxis(ap=start_i[0:TP, c:c + 1], axis=1)).then_inc(fields_in, 16)

            def gather(a, table):
                pool.wait_ge(table_out, TABLE_SUM[a])
                if a in (2, 3):
                    for u in range(2):
                        pool.wait_ge(rel_stored[u], 16 * PAIRS * (a - 1))
                first_tile = a * TILES

                def turn(i, first):
                    for j in range(U):
                        if j % RING == 0:
                            pool.wait_ge(idx_ready, i * 2 + (a * (TURNS + 1) * 2 + j // RING + 1))
                            pool.nop(nofuse=True)
                        if not first or j >= RING:
                            pool.wait_ge(tile_summed, i * U + (first_tile + j - RING + 1))
                            pool.nop(nofuse=True)
                        pool.indirect_dma_start(
                            out=rows[:, j % RING, :], out_offset=None, in_=table,
                            in_offset=bass.IndirectOffsetOnAxis(ap=idx_ring[:, j:j + 1], axis=0)).then_inc(gathered[j % RING], 16)

                if a == 0:
                    turn(0, True)
                with pool.Fori(1 if a == 0 else 0, TURNS) as i:
                    turn(i, False)

            for a in range(AGGS):
                if a > 0:
                    pool.wait_ge(acc_read, a)
                    pool.memset(acc[:, :], 0.0).then_inc(acc_zeroed, 1)
                if a in (2, 3):
                    gather(a, rel_table[a - 2].rearrange("n (r w) -> (n r) w", w=D))
                else:
                    gather(a, node_table[a])

        @block.scalar
        def _(act):
            step = Chain(act, act_step)
            pieces = QL // BPC
            for l in range(LAYERS):
                for c in range(pieces):
                    n = l * pieces + c
                    if n >= 2:
                        act.wait_ge(bases_out[n % 2], 16 * (n // 2))
                    for h in range(2):
                        act.wait_ge(bases_mixed, 2 * n + h + 1)
                        act.activation(base_out[:, n % 2, h * 512:(h + 1) * 512], ps[0:QB * RELS, (2 * n + h) % 4, :],
                                       ACT.Copy).then_inc(bases_copied, 1)
                    act.wait_ge(bases_copied, 2 * n + 2)
                    act.dma_start(rel_weight[l][:, c * BPC:(c + 1) * BPC], base_out[:, n % 2, :]).then_inc(bases_out[n % 2], 16)

            def root(n):
                act.wait_ge(var_ready, n)
                act.activation(small[:, 1, :], small[:, 0, :], ACT.Sqrt).then_inc(root_ready, 1)

            def norm_block(n, b, dest):
                act.nop(nofuse=True)
                act.activation(dest, blk(X, b), ACT.Relu, bias=shift[:, ds(b, 1)], scale=rstd[:, ds(b, 1)]).then_inc(normed, 1)

            def edges(a):
                table = rel_idx if a in (2, 3) else src_idx
                for h in range(2):
                    act.activation(idx_ring[:, h * RING:(h + 1) * RING], table[:, h * RING:(h + 1) * RING],
                                   ACT.Copy).then_inc(idx_ready, 1)
                with act.Fori(0, TURNS) as i:
                    if a in SELF_W:
                        s = SELF_BASE[a]
                        act.nop(nofuse=True)
                        act.activation(self_stage[:, :], blk(H, i), ACT.Copy).then_inc(self_staged, 1)
                    for h in range(2):
                        act.wait_ge(tile_summed, i * U + (a * TILES + (h + 1) * RING))
                        act.activation(idx_ring[:, h * RING:(h + 1) * RING],
                                       table[:, ds(i * U + (U + h * RING), RING)], ACT.Copy).then_inc(idx_ready, 1)
                        if a in SELF_W and h == 0:
                            act.wait_ge(self_transposed, i + (s + 1))
                            act.activation(self_turned[:, :], ps[:, 4, 0:D], ACT.Copy).then_inc(self_copied, 1)
                    if a in SELF_W:
                        act.wait_ge(self_multiplied, i + (s + 1))
                        act.nop(nofuse=True)
                        act.activation(blk(SELF, i), ps[:, 5, 0:D], ACT.Copy).then_inc(self_saved, 1)

            def turn_pair(i, name):
                for u in range(2):
                    act.wait_ge(transposed, i * 2 + (TURN_BASE[name] + u + 1))
                    act.activation(turned_sb[:, u, :], ps[:, 4 + u, 0:D], ACT.Copy).then_inc(turned, 1)

            def turn_pass(name):
                with act.Fori(0, PAIRS) as i:
                    turn_pair(i, name)

            def rel_pass(l):
                def body(i, first):
                    for u in range(2):
                        b = i * 2 + u
                        if l == 0:
                            norm_block(1, b, blk(H, b))
                        else:
                            act.wait_ge(pre_relu, i * 2 + (u + 1))
                            act.nop(nofuse=True)
                            act.activation(blk(H, b), tmp[:, u, :], ACT.Relu).then_inc(normed, 1)
                        act.wait_ge(normed, i * 2 + ((1 + l) * NB + u + 1))
                        act.nop(nofuse=True)
                        act.activation(stage[:, u, :], blk(H, b), ACT.Copy).then_inc(staged, 1)
                    turn_pair(i, f"r{l}")
                    for u in range(2):
                        act.wait_ge(rel_done, i * 4 + (2 * l * NB + 2 * u + 2))
                        if not first:
                            act.wait_ge(rel_stored[u], i * 16 + (16 * PAIRS * l))
                        act.activation(rel_rows[:, u, RELS * D // 2:].rearrange("p (a w) -> p a w", w=512),
                                       ps[:, 2:4, :], ACT.Copy).then_inc(rel_high_saved, 1)

                if l == 0:
                    body(0, True)
                with act.Fori(1 if l == 0 else 0, PAIRS) as i:
                    body(i, False)

            def norm_pass(n):
                with act.Fori(0, NB) as b:
                    norm_block(n, b, blk(H, b))

            root(1)
            act.wait_ge(norm_ready, 1)
            norm_pass(0)
            act.wait_ge(slots_made, 4)
            act.wait_ge(normed, NB)
            edges(0)
            turn_pass("p0")
            act.wait_ge(var_ready, 2)
            act.activation(small[:, 1, :], small[:, 0, :], ACT.Sqrt).then_inc(root_ready, 1)
            act.wait_ge(block_done, NB)
            edges(1)
            turn_pass("p1")
            root(3)
            act.wait_ge(norm_ready, 2)
            rel_pass(0)
            act.wait_ge(normed, 2 * NB)
            edges(2)
            rel_pass(1)
            act.wait_ge(normed, 3 * NB)
            edges(3)
            root(4)
            act.wait_ge(norm_ready, 3)
            norm_pass(2)
            edges(4)
            turn_pass("p4")
            edges(5)
            turn_pass("p5")
            root(5)
            act.wait_ge(norm_ready, 4)
            with act.Fori(0, PAIRS) as i:
                for u in range(2):
                    act.nop(nofuse=True)
                    act.activation(stage[:, u, :], blk(X, i * 2 + u), ACT.Relu, bias=shift[:, ds(i * 2 + u, 1)],
                                   scale=rstd[:, ds(i * 2 + u, 1)]).then_inc(staged, 1)
                turn_pair(i, "m")
            edges(6)

        @block.tensor
        def _(pe):
            pe.wait_ge(coef_in, 16 * LAYERS * QB)
            pieces = QL // BPC
            for l in range(LAYERS):
                for c in range(pieces):
                    n = l * pieces + c
                    pe.wait_ge(bases_in[n % 2], 16 * QB * (n // 2 + 1))
                    for h in range(2):
                        m = 2 * n + h
                        if m >= 4:
                            pe.wait_ge(bases_copied, m - 3)
                        pe.matmul(ps[0:QB * RELS, m % 4, :], coef[:, l, :], base_in[:, n % 2, h * 512:(h + 1) * 512],
                                  start=True, stop=True).then_inc(bases_mixed, 1)
            pe.wait_ge(counted, 1)
            pe.wait_ge(pool_step, 4)
            pe.matmul(ps[:, 5, 0:NB], ones[0:EP, :], cnt[0:EP, :], start=True, stop=True).then_inc(cum_made, 1)
            for f in range(FIELDS):
                pe.wait_ge(fields_made, f + 1)
                for c in range(TC):
                    last = pe.transpose(ps[:, 4 + f, c * TP:(c + 1) * TP], rec_f[f][:, c * P:(c + 1) * P],
                                        ident[0:TP, 0:TP])
                last.then_inc(fields_turned, 1)
            pe.wait_ge(weights_in, 16 * (len(WNAMES) + LAYERS + 4))
            pe.wait_ge(slots_made, 4)
            pe.wait_ge(bases_copied, 4 * pieces)

            def edges(a):
                first_tile = a * TILES

                def tile(i, j, first):
                    if not first or j >= BANKS:
                        pe.wait_ge(tile_added, i * U + (first_tile + j - BANKS + 1))
                    pe.wait_ge(gathered[j % RING], i * (16 * U // RING) + 16 * (a * TILES // RING + j // RING + 1))
                    pe.wait_ge(match_ready, i * U + (first_tile + j + 1))
                    s, k = j % BANKS, j % RING
                    last = pe.matmul(ps[:, s, 0:D], match[:, k, :], rows[:, k, :], start=True, stop=True)
                    if a == 0:
                        last = pe.matmul(ps[:, s, D:D + 2], match[:, k, :],
                                         ones_w[:, ds(i * U + j, 1), :].rearrange("p a c -> p (a c)"),
                                         start=True, stop=True)
                    last.then_inc(tile_summed, 1)

                def turn(i, first):
                    for j in range(U):
                        tile(i, j, first)
                        if a in SELF_W and j == 2:
                            s = SELF_BASE[a]
                            pe.wait_ge(self_staged, i + (s + 1))
                            for c in range(KC):
                                last = pe.transpose(ps[:, 4, c * P:(c + 1) * P], self_stage[:, c * P:(c + 1) * P], ident[:, :])
                            last.then_inc(self_transposed, 1)
                        if a in SELF_W and j == U - 4:
                            pe.wait_ge(self_copied, i + (s + 1))
                            for c in range(KC):
                                last = pe.matmul(ps[:, 5, 0:D], self_turned[:, c * P:(c + 1) * P], W[SELF_W[a]][:, c, :],
                                                 start=(c == 0), stop=(c == KC - 1 and a >= 2))
                            if a < 2:
                                last = pe.matmul(ps[:, 5, 0:D], ones[0:1, :], bias_row[0:1, a, :], start=False, stop=True)
                            last.then_inc(self_multiplied, 1)

                if a == 0:
                    turn(0, True)
                with pe.Fori(1 if a == 0 else 0, TURNS) as i:
                    turn(i, False)

            def transpose_pair(i, name):
                for u in range(2):
                    pe.wait_ge(staged, i * 2 + (TURN_BASE[name] + u + 1))
                    for c in range(KC):
                        last = pe.transpose(ps[:, 4 + u, c * P:(c + 1) * P], stage[:, u, c * P:(c + 1) * P], ident[:, :])
                    last.then_inc(transposed, 1)

            def project_pass(a):
                with pe.Fori(0, PAIRS) as i:
                    transpose_pair(i, f"p{a}")
                    for u in range(2):
                        pe.wait_ge(turned, i * 2 + (TURN_BASE[f"p{a}"] + u + 1))
                        for c in range(KC):
                            last = pe.matmul(ps[:, 6 + u, 0:D], turned_sb[:, u, c * P:(c + 1) * P], W[PROJECT_W[a]][:, c, :],
                                             start=(c == 0), stop=(c == KC - 1))
                        last.then_inc(multiplied, 1)

            def rel_pass(l):
                pe.wait_ge(wrel_in, 16 * QB * (l + 1))

                def body(i, first):
                    transpose_pair(i, f"r{l}")
                    for u in range(2):
                        pe.wait_ge(turned, i * 2 + (TURN_BASE[f"r{l}"] + u + 1))
                        for h in range(2):
                            if not first or u > 0:
                                pe.wait_ge((rel_low_saved, rel_high_saved)[h], i * 2 + (l * NB + u))
                            for g in range(2):
                                for c in range(KC):
                                    last = pe.matmul(ps[:, 2 * h + g, :], turned_sb[:, u, c * P:(c + 1) * P],
                                                     Wrel[:, c, (2 * h + g) * 512:(2 * h + g + 1) * 512],
                                                     start=(c == 0), stop=(c == KC - 1))
                            last.then_inc(rel_done, 1)

                if l == 0:
                    body(0, True)
                with pe.Fori(1 if l == 0 else 0, PAIRS) as i:
                    body(i, False)

            def maxk_pass():
                with pe.Fori(0, PAIRS) as i:
                    transpose_pair(i, "m")
                    for u in range(2):
                        pe.wait_ge(turned, i * 2 + (TURN_BASE["m"] + u + 1))
                        pe.wait_ge(scaled, i * 2 + (2 * NB + u - 1))
                        for c in range(KC):
                            pe.matmul(ps[:, 6 + u, 0:D], turned_sb[:, u, c * P:(c + 1) * P], W["L3_gnn_W_neigh"][:, c, :],
                                      start=(c == 0), stop=(c == KC - 1))
                        for c in range(KC):
                            last = pe.matmul(ps[:, u, 0:D], turned_sb[:, u, c * P:(c + 1) * P], W["L3_gnn_W_self"][:, c, :],
                                             start=(c == 0), stop=(c == KC - 1))
                        last.then_inc(multiplied, 1)

            edges(0)
            project_pass(0)
            edges(1)
            project_pass(1)
            rel_pass(0)
            edges(2)
            rel_pass(1)
            edges(3)
            edges(4)
            project_pass(4)
            edges(5)
            project_pass(5)
            maxk_pass()
            edges(6)

        @block.vector
        def _(v):
            step = Chain(v, dve_step)
            full = BLOCKS - 1
            v.memset(X[:, full * D:NB * D], 0.0).then_inc(const_made, 1)
            v.memset(coef[:, :, :], 0.0).then_inc(const_made, 1)
            step(v.memset(ones[:, :], 1.0))
            step(v.memset(ones_w[:, :, :], 1.0))
            step(v.memset(src_idx[:, :], 0))
            step(v.memset(rel_idx[:, :], 0))
            v.wait_ge(dst_in, 16)
            step(v.tensor_copy(dst_f, dst_i))
            for b in range(NB):
                step(v.tensor_scalar(below, dst_f, float((b + 1) * P), None, ALU.is_lt, ALU.add,
                                     accum_out=cnt[0:EP, b:b + 1]))
            v.drain().then_inc(counted, 1)

            def stats_of(b, u, row):
                v.nop(nofuse=True)
                step(v.bn_stats(stats[:, u, :], row))
                v.nop(nofuse=True)
                step(v.bn_aggr(mv_pair[:, u, :], stats[:, u, :]))
                v.nop(nofuse=True)
                step(v.tensor_copy(mv[:, ds(b * 2, 2)], mv_pair[:, u, :]))

            def add_to_x(b, u, term):
                step(v.tensor_tensor(tmp2[:, u, :], blk(X, b), term, ALU.add))
                v.nop(nofuse=True)
                step(v.tensor_copy(blk(X, b), tmp2[:, u, :]))
                stats_of(b, u, tmp2[:, u, :])

            mv_of = mv.rearrange("p (b c) -> p b c", c=2)

            def finish_norm(n):
                v.tensor_scalar(small[:, 0, :], mv_of[:, :, 1], EPS, None, ALU.add).then_inc(var_ready, 1)
                v.wait_ge(root_ready, n)
                step(v.reciprocal(rstd[:, :], small[:, 1, :]))
                step(v.tensor_tensor(small[:, 1, :], rstd[:, :], rstd[:, :], ALU.mult))
                step(v.tensor_tensor(small[:, 1, :], small[:, 1, :], small[:, 0, :], ALU.mult))
                step(v.tensor_scalar(small[:, 1, :], small[:, 1, :], -0.5, 1.5, ALU.mult, ALU.add))
                step(v.tensor_tensor(rstd[:, :], rstd[:, :], small[:, 1, :], ALU.mult))
                step(v.tensor_scalar(shift[:, :], mv_of[:, :, 0], -1.0, None, ALU.mult))
                v.tensor_tensor(shift[:, :], shift[:, :], rstd[:, :], ALU.mult).then_inc(norm_ready, 1)

            v.wait_ge(nodes_in, 32)
            
            def first_stats(b):
                v.nop(nofuse=True)
                step(v.tensor_copy(tmp2[:, 0, :], blk(X, b)))
                stats_of(b, 0, tmp2[:, 0, :])

            step.loop(0, NB, 4, first_stats)
            finish_norm(1)

            v.wait_ge(pool_step, 4)
            v.wait_ge(cum_made, 1)
            step(v.tensor_copy(cum[:, :], ps[:, 5, 0:NB]))
            n_, t_, ts, pad_, nxt, m_ = (runs[:, k, :] for k in range(6))
            B = slice(0, BLOCKS)
            step(v.tensor_copy(n_[:, 0:1], cum[:, 0:1]))
            step(v.tensor_tensor(n_[:, 1:NB], cum[:, 1:NB], cum[:, 0:NB - 1], ALU.subtract))
            step(v.tensor_scalar(t_, n_, float(P - 1), None, ALU.add))
            step(v.tensor_copy(runs_i[:, :], t_))
            step(v.tensor_scalar(runs_i[:, :], runs_i[:, :], 7, None, ALU.arith_shift_right))
            step(v.tensor_copy(t_, runs_i[:, :]))
            step(v.memset(m_, 0.0))
            step(v.tensor_tensor_scan(ts, t_, m_, 0.0, ALU.add, ALU.add))
            step(v.scalar_tensor_tensor(pad_, t_, float(P), n_, ALU.mult, ALU.subtract))
            step(v.tensor_copy(nxt[:, B], n_[:, 1:NB]))
            blk_, lost, end_, start_, first_, lo, hi, rel = (cut[0:TP, k, :] for k in range(8))
            for c in range(TC):
                k = tile_no[0:TP, c:c + 1]
                for dest, other in ((blk_, None), (lost, pad_), (end_, nxt)):
                    if other is None:
                        step(v.tensor_scalar(m_[0:TP, B], ts[0:TP, B], k, None, ALU.is_le, ALU.add, accum_out=dest[:, c:c + 1]))
                    else:
                        step(v.scalar_tensor_tensor(m_[0:TP, B], ts[0:TP, B], k, other[0:TP, B], ALU.is_le, ALU.mult,
                                                    accum_out=dest[:, c:c + 1]))
            step(v.tensor_scalar(end_, end_, n_[0:TP, 0:1], None, ALU.add))
            step(v.scalar_tensor_tensor(first_, tile_no[0:TP, :], float(P), lost, ALU.mult, ALU.subtract))
            step(v.tensor_scalar(start_, first_, float(EDGES - P), None, ALU.min))
            step(v.tensor_copy(start_i[0:TP, :], start_))
            step(v.tensor_scalar(rel, blk_, float(AW), None, ALU.mult))
            v.tensor_copy(acc_i[0:TP, :], rel).then_inc(starts_made, 1)
            v.drain().then_inc(starts_made, 1)
            step(v.tensor_tensor(lo, first_, start_, ALU.subtract))
            step(v.tensor_tensor(hi, end_, start_, ALU.subtract))
            step(v.tensor_scalar(rel, blk_, -float(P), 1.0, ALU.mult, ALU.add))
            for c in range(TC):
                vc = valid[:, c * P:(c + 1) * P]
                step(v.tensor_scalar(vc, column[0:TP, :], lo[:, c:c + 1], None, ALU.is_ge))
                step(v.scalar_tensor_tensor(vc, column[0:TP, :], hi[:, c:c + 1], vc, ALU.is_lt, ALU.mult))
            v.wait_ge(fields_in, 16 * FIELDS * TC)
            for f in range(3):
                step(v.tensor_copy(rec_f[f][:, :], rec[f].bitcast(i32)))
            for c in range(TC):
                rc = rec_f[0][:, c * P:(c + 1) * P]
                step(v.scalar_tensor_tensor(rc, rc, rel[:, c:c + 1], valid[:, c * P:(c + 1) * P], ALU.add, ALU.mult))
            step(v.scalar_tensor_tensor(rec_f[2], rec_f[1], float(RELS), rec_f[2], ALU.mult, ALU.add))
            v.tensor_copy(rec_f[3], rec[3]).then_inc(fields_made, 4)

            def by_tile(f):
                return ps[:, 4 + f, 0:TILES].rearrange("e (c p) -> e p c", c=TC)

            v.wait_ge(fields_turned, 4)
            v.tensor_scalar(target.rearrange("e (p c) -> e p c", c=TC), by_tile(0), -1.0, None, ALU.add).then_inc(slots_made, 1)
            v.tensor_copy(src_idx[:, 0:TILES].rearrange("e (p c) -> e p c", c=TC), by_tile(1)).then_inc(slots_made, 1)
            v.tensor_copy(rel_idx[:, 0:TILES].rearrange("e (p c) -> e p c", c=TC), by_tile(2)).then_inc(slots_made, 1)
            v.tensor_copy(ones_w[:, :, 1].rearrange("e (p c) -> e p c", c=TC), by_tile(3)).then_inc(slots_made, 1)
            v.wait_ge(tile_acc_in, 16)
            v.wait_ge(slots_made, 4)

            def edges(a):
                first_tile = a * TILES
                width = D + 2 if a == 0 else D
                v.wait_ge(acc_zeroed, a + 1)

                def turn(i, first):
                    _, col = nc.values_load_multi_w_load_instructions(
                        tile_acc[0:1, ds(i * U, U)], engines=[DVE], min_val=0, max_val=BLOCKS * AW,
                        skip_runtime_bounds_check_because="made on the chip from at most BLOCKS runs")
                    for j in range(U + LEAD):
                        if j < U:
                            if not first or j >= RING:
                                v.wait_ge(tile_summed, i * U + (first_tile + j - RING + 1))
                            k = i * U + j
                            if a in (4, 5):
                                v.tensor_scalar(match[:, j % RING, :], column[:, :], target[:, ds(k, 1)],
                                                ones_w[:, ds(k, 1), 1], ALU.is_equal, ALU.mult).then_inc(match_ready, 1)
                            else:
                                v.tensor_scalar(match[:, j % RING, :], column[:, :], target[:, ds(k, 1)], None,
                                                ALU.is_equal).then_inc(match_ready, 1)
                        if j >= LEAD:
                            q = j - LEAD
                            v.wait_ge(tile_summed, i * U + (first_tile + q + 1))
                            if not first or q > 0:
                                v.wait_ge(tile_added, i * U + (first_tile + q))
                            sums = acc[:, ds(col[q], width)]
                            v.tensor_tensor(sums, sums, ps[:, q % BANKS, 0:width], ALU.add).then_inc(tile_added, 1)

                if a == 0:
                    turn(0, True)
                with v.Fori(1 if a == 0 else 0, TURNS) as i:
                    turn(i, False)
                v.wait_ge(tile_added, (a + 1) * TILES)

            def sums_of(b):
                return acc[:, ds(b * AW, D)]

            def scale(tensor, b):
                return tensor[:, ds(b, 1)]

            def mean_pair(i):
                for u in range(2):
                    b = i * 2 + u
                    v.tensor_scalar(stage[:, u, :], sums_of(b), scale(rdeg, b), None, ALU.mult).then_inc(staged, 1)

            edges(0)
            deg = acc.rearrange("p (b w) -> p b w", w=AW)
            step(v.tensor_scalar(rdeg[:, :], deg[:, :, D], 1.0, None, ALU.max))
            step(v.reciprocal(rdeg[:, :], rdeg[:, :]))
            step(v.tensor_scalar(dinv[:, :], deg[:, :, D + 1], 1.0, None, ALU.add))
            step(v.tensor_scalar(shift[:, :], dinv[:, :], 0.0, None, ALU.is_gt))
            v.tensor_scalar(small[:, 0, :], dinv[:, :], 1e-30, None, ALU.max).then_inc(var_ready, 1)

            def sage_pass(a):
                v.wait_ge(self_saved, SELF_BASE[a] + NB)

                def body(i):
                    mean_pair(i)
                    for u in range(2):
                        b = i * 2 + u
                        v.wait_ge(multiplied, i * 2 + (MUL_BASE[f"p{a}"] + u + 1))
                        step(v.tensor_tensor(tmp[:, u, :], ps[:, 6 + u, 0:D], blk(SELF, b), ALU.add))
                        if a == 0:
                            v.tensor_scalar(blk(H, b), tmp[:, u, :], 0.0, None, ALU.max).then_inc(block_done, 1)
                        else:
                            add_to_x(b, u, tmp[:, u, :])

                step.loop(0, PAIRS, 2 if a == 0 else 12, body)
                v.drain().then_inc(acc_read, 1)

            sage_pass(0)
            v.wait_ge(root_ready, 2)
            step(v.reciprocal(dinv[:, :], small[:, 1, :]))
            step(v.tensor_tensor(small[:, 1, :], dinv[:, :], dinv[:, :], ALU.mult))
            step(v.tensor_tensor(small[:, 1, :], small[:, 1, :], small[:, 0, :], ALU.mult))
            step(v.tensor_scalar(small[:, 1, :], small[:, 1, :], -0.5, 1.5, ALU.mult, ALU.add))
            step(v.tensor_tensor(dinv[:, :], dinv[:, :], small[:, 1, :], ALU.mult))
            step(v.tensor_tensor(dinv[:, :], dinv[:, :], shift[:, :], ALU.mult))
            edges(1)
            sage_pass(1)
            finish_norm(3)

            def rel_low(l):
                def body(i, first):
                    if l == 1:
                        for u in range(2):
                            b = i * 2 + u
                            v.scalar_tensor_tensor(tmp[:, u, :], sums_of(b), scale(rdeg, b), blk(SELF, b),
                                                   ALU.mult, ALU.add).then_inc(pre_relu, 1)
                    for u in range(2):
                        v.wait_ge(rel_done, i * 4 + (2 * l * NB + 2 * u + 1))
                        if not first:
                            v.wait_ge(rel_stored[u], i * 16 + (16 * PAIRS * l))
                        v.tensor_copy(rel_rows[:, u, 0:RELS * D // 2].rearrange("p (a w) -> p a w", w=512),
                                      ps[:, 0:2, :]).then_inc(rel_low_saved, 1)

                if l == 0:
                    body(0, True)
                with v.Fori(1 if l == 0 else 0, PAIRS) as i:
                    body(i, False)

            rel_low(0)
            edges(2)
            v.wait_ge(self_saved, SELF_BASE[2] + NB)
            rel_low(1)
            v.drain().then_inc(acc_read, 1)
            edges(3)
            v.wait_ge(self_saved, SELF_BASE[3] + NB)

            def rgcn_out(i):
                for u in range(2):
                    b = i * 2 + u
                    step(v.scalar_tensor_tensor(tmp[:, u, :], sums_of(b), scale(rdeg, b), blk(SELF, b), ALU.mult, ALU.add))
                    add_to_x(b, u, tmp[:, u, :])

            step.loop(0, PAIRS, 12, rgcn_out)
            v.drain().then_inc(acc_read, 1)
            finish_norm(4)

            with v.Fori(0, PAIRS) as i:
                for u in range(2):
                    b = i * 2 + u
                    v.wait_ge(normed, i * 2 + (3 * NB + u + 1))
                    if u == 0:
                        v.wait_ge(table_out, i * 16 + TABLE_SUM[1])
                    v.tensor_scalar(tmp2[:, u, :], blk(H, b), scale(dinv, b), None, ALU.mult).then_inc(scaled, 1)
            edges(4)

            def gcn_pass(a):
                def body(i):
                    for u in range(2):
                        b = i * 2 + u
                        step(v.scalar_tensor_tensor(tmp[:, u, :], blk(H, b), scale(dinv, b), sums_of(b), ALU.mult, ALU.add))
                        v.tensor_scalar(stage[:, u, :], tmp[:, u, :], scale(dinv, b), None, ALU.mult).then_inc(staged, 1)
                    for u in range(2):
                        b = i * 2 + u
                        v.wait_ge(multiplied, i * 2 + (MUL_BASE[f"p{a}"] + u + 1))
                        step(v.tensor_tensor(tmp[:, u, :], ps[:, 6 + u, 0:D], bias[:, a - 4, :], ALU.add))
                        step(v.tensor_scalar(blk(H, b), blk(H, b), PRESERVE, None, ALU.mult))
                        step(v.scalar_tensor_tensor(blk(H, b), tmp[:, u, :], 1.0 - PRESERVE, blk(H, b), ALU.mult, ALU.add))
                        if a == 4:
                            if u == 0:
                                v.wait_ge(table_out, i * 16 + TABLE_SUM[4])
                            v.tensor_scalar(tmp2[:, u, :], blk(H, b), scale(dinv, b), None, ALU.mult).then_inc(scaled, 1)
                        else:
                            add_to_x(b, u, blk(H, b))

                step.loop(0, PAIRS, 8 if a == 4 else 18, body)
                v.drain().then_inc(acc_read, 1)

            gcn_pass(4)
            edges(5)
            gcn_pass(5)
            finish_norm(5)

            GONE = -3.0e38

            def maxk(i):
                for u in range(2):
                    b = i * 2 + u
                    v.wait_ge(multiplied, i * 2 + (MUL_BASE["m"] + u + 1))
                    step(v.tensor_tensor(blk(X, b), blk(X, b), ps[:, u, 0:D], ALU.add))
                    step(v.tensor_copy(H[:, 0:D], ps[:, 6 + u, 0:D]))
                    for r in range(MAXK // 8):
                        v.nop(nofuse=True)
                        step(v.max(top8[:, :], H[:, 0:D]))
                        v.nop(nofuse=True)
                        step(v.match_replace(H[:, 0:D], top8[:, :], H[:, 0:D], GONE))
                    step(v.tensor_scalar(H[:, 0:D], H[:, 0:D], GONE, None, ALU.is_equal))
                    if u == 0:
                        v.wait_ge(table_out, i * 16 + TABLE_SUM[5])
                    v.tensor_tensor(tmp2[:, u, :], H[:, 0:D], ps[:, 6 + u, 0:D], ALU.mult).then_inc(scaled, 1)

            step.loop(0, PAIRS, 2 * (3 + MAXK // 8 * 2), maxk)
            edges(6)
            with v.Fori(0, PAIRS) as i:
                for u in range(2):
                    b = i * 2 + u
                    v.scalar_tensor_tensor(blk(X, b), sums_of(b), scale(rdeg, b), blk(X, b), ALU.mult,
                                           ALU.add).then_inc(block_done, 1)


_INS = ['x', 'src', 'dst', 'edge_type_8', 'edge_weight', 'L0_gnn_W1_l', 'L0_gnn_b1', 'L0_gnn_W1_r', 'L0_gnn_W2_l',
        'L0_gnn_b2', 'L0_gnn_W2_r', 'L1_gnn_bases', 'L1_gnn_coeffs', 'L1_gnn_self_loops', 'L2_gnn_W1', 'L2_gnn_b1',
        'L2_gnn_W2', 'L2_gnn_b2', 'L3_gnn_W_self', 'L3_gnn_W_neigh']


def kernel(**inputs):
    import numpy as _np
    import concourse.bacc as _bacc
    from concourse import mybir as _mybir
    from concourse.bass_utils import run_bass_kernel_spmd as _run

    nc = _bacc.Bacc("TRN2", target_bir_lowering=False, num_devices=1)
    arrays, tensors = {}, {}
    for name in _INS:
        a = _np.ascontiguousarray(inputs[name])
        arrays[f"in_{name}"] = a
        tensors[name] = nc.dram_tensor(f"in_{name}", a.shape, _mybir.dt.from_np(a.dtype), kind="ExternalInput").ap()
    out = nc.dram_tensor("out", arrays["in_x"].shape, _mybir.dt.float32, kind="ExternalOutput").ap()
    gnn_program(nc, tensors, out)
    r = _run(nc, [arrays], core_ids=[0])
    return r.results[0]["out"]
```
